# Optimizing a Trainium2 kernel written in Bass

```python
import numpy as np
import jax
import jax.numpy as jnp

def _softmax(x, axis=-1):
    return jax.nn.softmax(x, axis=axis)
def _gelu(x):
    return jax.nn.gelu(x, approximate=True)
def _silu(x):
    return jax.nn.silu(x)
def _sigmoid(x):
    return jax.nn.sigmoid(x)
def _layernorm(x, axis=-1, eps=1e-5):
    m = jnp.mean(x, axis=axis, keepdims=True)
    v = jnp.var(x, axis=axis, keepdims=True)
    return (x - m) / jnp.sqrt(v + eps)
def _scatter_add(tgt, idx, src, axis=0):
    return tgt.at[idx].add(src)
def _segment_sum(src, seg, n):
    return jax.ops.segment_sum(src, seg, n)

kernel_name = 'mk_adj_resnorm_d1_adj_128_955b45'

def setup_inputs(seed: int = 0):
    np.random.seed(seed)
    _w = jnp.asarray
    def _rec_inputs():
        import jax
        import jax.numpy as jnp
        _gk = jax.random.key(seed)
        x = -0.000929 + 1 * jax.random.normal(jax.random.fold_in(_gk, 1), (8192, 128), jnp.float32)
        _w = (1.0 + jnp.arange(8192, dtype=jnp.float32)) ** -0.5
        _w = _w / _w.mean()
        _pij = jnp.clip(0.000976562 * _w[:, None] * _w[None, :], 0.0, 1.0)
        _a = jax.random.uniform(jax.random.fold_in(_gk, 2), (8192, 8192)) < _pij
        adj = _a.astype(jnp.int32)
        return x, adj
    x, adj = _rec_inputs()
    def _L0_gnn_setup():
        import jax, jax.numpy as jnp
        import numpy as np
        NEG_INF = -1000000000.0
        key = jax.random.key(seed)
        k1, k2, k3, k4 = jax.random.split(key, 4)
        N, Fin, Fout = (8192, 128, 128)
        h = jax.random.normal(k1, (N, Fin), dtype=jnp.float32)
        adj = jax.random.randint(k2, (N, N), 0, 2, dtype=jnp.int32)
        W = jax.random.normal(k3, (Fin, Fout), dtype=jnp.float32) * (1.0 / np.sqrt(Fin))
        a = jax.random.normal(k4, (2 * Fout,), dtype=jnp.float32) * (1.0 / np.sqrt(2 * Fout))
        return {'h': h, 'adj': adj, 'W': W, 'a': a}
    _L0_gnn_all = _L0_gnn_setup()
    _L0_gnn_in = {k: v for k, v in _L0_gnn_all.items() if k in ('W', 'a', )}
    del _L0_gnn_all

    return {
        "x": x,
        "adj": adj,
        "L0_gnn_W": _L0_gnn_in["W"],
        "L0_gnn_a": _L0_gnn_in["a"],
    }

def reference(x, adj, L0_gnn_W, L0_gnn_a):
    import jax
    import jax.numpy as jnp
    def _L0_gnn_ref(h, adj, W, a):
        import jax, jax.numpy as jnp
        import numpy as np
        NEG_INF = -1000000000.0
        Fout = W.shape[1]
        Wh = h @ W
        a1, a2 = (a[:Fout], a[Fout:])
        s_key = Wh @ a1
        s_qry = Wh @ a2
        e = jax.nn.leaky_relu(s_qry[:, None] + s_key[None, :], negative_slope=0.2)
        scores = jnp.where(adj > 0, e, jnp.float32(NEG_INF))
        attention = jax.nn.softmax(scores, axis=1)
        h_prime = attention @ Wh
        return jax.nn.elu(h_prime)

    x = _layernorm(x + _L0_gnn_ref(x, adj, L0_gnn_W, L0_gnn_a), axis=-1)
    return x


_drawn_inputs = setup_inputs


def setup_inputs(seed=0):
    import zlib

    import numpy as np

    out = dict(_drawn_inputs(seed))
    spreads = {}
    factors = {}
    for name, (base, spread) in spreads.items():
        noise = np.random.default_rng([zlib.crc32(name.encode()), seed]).standard_normal(out[name].shape)
        drawn = base * np.exp(spread * noise) if base else spread * noise
        out[name] = jnp.asarray(drawn.astype(out[name].dtype))
    for name, factor in factors.items():
        out[name] = (out[name] * factor).astype(out[name].dtype)
    return out
```

```python
from contextlib import ExitStack

import concourse.bass as bass
from concourse import mybir


def build(nc, xT, x, adjT, W, WT, a, out):
    F32, BF16, I32 = mybir.dt.float32, mybir.dt.bfloat16, mybir.dt.int32
    ALU, ACT, AX = mybir.AluOpType, mybir.ActivationFunctionType, mybir.AxisListType

    P = 128
    N, D = x.shape
    GQ = 1024
    NG = N // GQ
    T = GQ // P
    NB = N // P
    BPC = 2
    SLOTS = 4
    BPS = BPC * SLOTS
    SPG = NB // BPS
    STEPS = NG * SPG
    E = D + 1
    QC = 512
    CPQ = 4
    QUARTERS = N // (QC * CPQ)
    KPP = QC // P
    SLOPE = 0.8
    OPEN = 2.0 ** 96
    LIMIT = 2.0 ** 95
    EPS = 1e-5

    ctx = ExitStack()
    with ctx:
        def sb(name, shape, dt=F32):
            return ctx.enter_context(nc.sbuf_tensor(name, shape, dt))

        def sem(name):
            return ctx.enter_context(nc.semaphore(name))

        w_ext = sb("w_ext", [P, E])
        w_t = sb("w_t", [P, D])
        a_t = sb("a_t", [P, 2])
        wa2 = sb("wa2", [P, P])
        r_all = sb("r_all", [P, N])
        v_all = sb("v_all", [P, NB, E])
        kcol = sb("kcol", [P, NB])
        bcol = sb("bcol", [P, NB])
        ucol = sb("ucol", [P, NB])
        kmax_p = sb("kmax_p", [P, 1])
        kmax = sb("kmax", [P, 1])
        rbias = sb("rbias", [P, 1])
        xsum_q = sb("xsum_q", [P, QUARTERS])
        xsum = sb("xsum", [P, 1])
        xmean = sb("xmean", [P, P])
        wh_mean = sb("wh_mean", [P, D])
        eps = sb("eps", [P, 1])
        adj = sb("adj", [P, SLOTS, BPC * GQ], I32)
        mask = sb("mask", [P, SLOTS, BPC * GQ], BF16)
        wts = sb("wts", [P, BPS, GQ])
        x_t = wts[:, :, :].rearrange("p b q -> p (b q)")
        x_res = sb("x_res", [P, 2, GQ])
        h = sb("h", [P, GQ])
        neg = sb("neg", [P, GQ])
        y = sb("y", [P, GQ])
        o = sb("o", [P, 2, GQ])
        den = sb("den", [P, T])
        lone = sb("lone", [P, T])
        rden = sb("rden", [P, T])
        stats = sb("stats", [P, T, 6])
        msum = sb("msum", [P, T])
        mdif = sb("mdif", [P, T])
        qsum = sb("qsum", [P, T])
        mean = sb("mean", [P, T])
        var = sb("var", [P, T])
        std = sb("std", [P, T])
        rstd = sb("rstd", [P, T])
        acc = [ctx.enter_context(nc.psum_tensor(f"acc{i}", [P, T, 256], F32)) for i in range(2)]

        s_w = sem("weights_loaded")
        s_xt = [sem(f"xT_loaded{i}") for i in range(QUARTERS)]
        s_adj = [sem(f"adj_loaded{i}") for i in range(SLOTS)]
        s_wa = sem("wa_in_psum")
        s_wext = sem("w_ext_ready")
        s_whp = sem("wh_piece_in_psum")
        s_qp = sem("q_piece_in_psum")
        s_whc = sem("wh_piece_copied")
        s_qc = sem("q_piece_copied")
        s_kp = sem("kmax_of_partitions")
        s_km = sem("kmax_ready")
        s_kc = sem("kprime_ready")
        s_bu = sem("b_and_u_ready")
        s_re = sem("r_exponential_ready")
        s_v = sem("v_scaled")
        s_xm = sem("xmean_ready")
        s_mp = sem("wh_mean_in_psum")
        s_pre = sem("vector_prologue_steps")
        s_mask = sem("masks_ready")
        s_wts = sem("weight_tiles_ready")
        s_used = sem("weight_tiles_used")
        s_epi = sem("vector_epilogue_steps")
        s_neg = sem("neg_ready")
        s_exp = sem("exp_ready")
        s_var = sem("variance_ready")
        s_std = sem("std_ready")
        s_xr = [sem(f"x_res_loaded{i}") for i in range(2)]
        s_o = sem("out_tile_ready")
        s_st = [sem(f"out_stored{i}") for i in range(2)]

        block = ctx.enter_context(nc.Block())

        @block.sync
        def _(sp):
            sp.dma_start(w_t[:, :], WT).then_inc(s_w, 16)
            sp.dma_start(a_t[:, :], a).then_inc(s_w, 16)
            sp.dma_start(w_ext[:, 0:D], W).then_inc(s_w, 16)
            for i in range(QUARTERS):
                n = N // QUARTERS
                sp.dma_start(x_t[:, i * n:(i + 1) * n], xT[:, i * n:(i + 1) * n]).then_inc(s_xt[i], 16)
            for c in range(SLOTS):
                sp.dma_start(adj[:, c, :], adjT[c, :, :]).then_inc(s_adj[c], 16)
            with sp.Fori(1, STEPS) as s:
                for c in range(SLOTS):
                    sp.wait_ge(s_mask, SLOTS * s + (c - SLOTS + 1))
                    sp.dma_start(adj[:, c, :], adjT[bass.ds(SLOTS * s + c, 1), :, :].rearrange("o p n -> (o p) n"))\
                        .then_inc(s_adj[c], 16)

        @block.gpsimd
        def _(pool):
            pool.wait_ge(s_kp, 1)
            nc.gpsimd.partition_all_reduce(kmax[:, :], kmax_p[:, :], P, bass.bass_isa.ReduceOp.max).then_inc(s_km, 1)
            pool.wait_ge(s_bu, 1)
            for s in range(SPG):
                v = v_all[:, s * BPS:(s + 1) * BPS, :]
                nc.gpsimd.tensor_tensor(v, v, bcol[:, s * BPS:(s + 1) * BPS].unsqueeze(2).to_broadcast([P, BPS, E]),
                                        ALU.mult).then_inc(s_v, 1)

            xg = x.rearrange("(g t p) d -> g p t d", t=T, p=P)
            og = out.rearrange("(g t p) d -> g p t d", t=T, p=P)

            def load(par, g):
                pool.dma_start(x_res[:, par, :].rearrange("p (t d) -> p t d", d=D),
                               xg[bass.ds(g, 1), :, :, :].rearrange("o p t d -> (o p) t d")).then_inc(s_xr[par], 16)

            def store(par, g):
                pool.wait_ge(s_o, g + 1)
                pool.dma_start(og[bass.ds(g, 1), :, :, :].rearrange("o p t d -> (o p) t d"),
                               o[:, par, :].rearrange("p (t d) -> p t d", d=D)).then_inc(s_st[par], 16)

            load(0, 0)
            load(1, 1)
            with pool.Fori(0, NG // 2 - 1) as gp:
                for par in range(2):
                    store(par, 2 * gp + par)
                    pool.wait_ge(s_var, 2 * gp + (par + 1))
                    load(par, 2 * gp + (par + 2))
            for par in range(2):
                store(par, NG - 2 + par)
            for par in range(2):
                pool.wait_ge(s_st[par], 16 * (NG // 2))

        @block.scalar
        def _(act):
            for n in range(QUARTERS * CPQ):
                act.wait_ge(s_qp, n + 1)
                nc.scalar.copy(r_all[:, n * QC:(n + 1) * QC], acc[1][:, 2 * (n % 4):2 * (n % 4) + 2, :]
                               .rearrange("p t c -> p (t c)")).then_inc(s_qc, 1)
            act.wait_ge(s_kc, 1)
            nc.scalar.activation(bcol[:, :], kcol[:, :], ACT.Exp)
            nc.scalar.activation(ucol[:, :], kcol[:, :], ACT.Exp, scale=-SLOPE).then_inc(s_bu, 1)
            act.wait_ge(s_qc, QUARTERS * CPQ)
            for i in range(SLOTS):
                r = r_all[:, i * (N // SLOTS):(i + 1) * (N // SLOTS)]
                nc.scalar.activation(r, r, ACT.Exp, bias=rbias[:, :], scale=SLOPE).then_inc(s_re, 1)

            def masks(s, first=False):
                for c in range(SLOTS):
                    act.wait_ge(s_adj[c], 16 * s + 16)
                    if not first:
                        act.wait_ge(s_wts, BPS * s + (BPC * (c + 1) - BPS))
                    nc.scalar.activation(mask[:, c, :], adj[:, c, :], ACT.Relu, scale=OPEN).then_inc(s_mask, 1)

            def exp_part(g):
                act.wait_ge(s_neg, g + 1)
                nc.scalar.activation(neg[:, :], neg[:, :], ACT.Exp).then_inc(s_exp, 1)

            def std_part(g):
                act.wait_ge(s_var, g + 1)
                nc.scalar.activation(std[:, :], var[:, :], ACT.Sqrt, bias=eps[:, :]).then_inc(s_std, 1)

            masks(0, first=True)
            with act.Fori(1, SPG) as s:
                masks(s)
            with act.Fori(1, NG) as g:
                for k in range(3):
                    masks(SPG * g + k)
                exp_part(g - 1)
                masks(SPG * g + 3)
                std_part(g - 1)
                with act.Fori(4, SPG) as k:
                    masks(SPG * g + k)
            exp_part(NG - 1)
            std_part(NG - 1)

        @block.vector
        def _(dve):
            steps = [0]

            def after(ins):
                steps[0] += 1
                ins.then_inc(s_pre, 1)
                dve.wait_ge(s_pre, steps[0])

            nc.vector.memset(eps[:, :], EPS)
            dve.wait_ge(s_w, 48)
            dve.wait_ge(s_wa, 1)
            nc.vector.tensor_copy(w_ext[:, D:E], acc[0][:, 0, 0:1])
            nc.vector.tensor_copy(wa2[:, :], acc[0][:, 0, 1:2].to_broadcast([P, P])).then_inc(s_wext, 1)
            for n in range(QUARTERS * CPQ):
                dve.wait_ge(s_whp, n + 1)
                nc.vector.tensor_copy(v_all[:, n * KPP:(n + 1) * KPP, :],
                                      acc[0][:, KPP * (n % 2):KPP * (n % 2) + KPP, 0:E]).then_inc(s_whc, 1)
                if n % CPQ == CPQ - 1:
                    i = n // CPQ
                    dve.wait_ge(s_xt[i], 16)
                    after(nc.vector.reduce_sum(xsum_q[:, i:i + 1], x_t[:, i * QC * CPQ:(i + 1) * QC * CPQ], AX.X))
            dve.wait_ge(s_whc, QUARTERS * CPQ)
            nc.vector.reduce_max(kmax_p[:, :], v_all[:, :, D], AX.X).then_inc(s_kp, 1)
            after(nc.vector.reduce_sum(xsum[:, :], xsum_q[:, :], AX.X))
            nc.vector.tensor_scalar(xmean[:, :], xsum[:, 0:1].to_broadcast([P, P]), 1.0 / N, None, ALU.mult)\
                .then_inc(s_xm, 1)
            dve.wait_ge(s_km, 1)
            nc.vector.tensor_scalar(rbias[:, :], kmax[:, :], SLOPE, None, ALU.mult)
            after(nc.vector.tensor_scalar(kcol[:, :], v_all[:, :, D], kmax[:, 0:1], None, ALU.subtract))
            nc.vector.memset(v_all[:, :, D:E], 1.0).then_inc(s_kc, 1)
            dve.wait_ge(s_bu, 1)
            nc.vector.tensor_scalar(ucol[:, :], ucol[:, :], LIMIT, None, ALU.min)
            for i in range(SLOTS):
                r = r_all[:, i * (N // SLOTS):(i + 1) * (N // SLOTS)]
                dve.wait_ge(s_re, i + 1)
                nc.vector.tensor_scalar(r, r, LIMIT, None, ALU.min)
            dve.wait_ge(s_mp, 1)
            after(nc.vector.tensor_copy(wh_mean[:, :], acc[1][:, 0, 0:D]))

            def weights(g, k, first=False):
                s = SPG * g + k
                for b in range(BPS):
                    if b % BPC == 0:
                        dve.wait_ge(s_mask, SLOTS * s + (b // BPC + 1))
                    if not first:
                        dve.wait_ge(s_used, BPS * s + (b - BPS + 1))
                    nc.vector.scalar_tensor_tensor(
                        out=wts[:, b, :], in0=r_all[:, bass.ds(g * GQ, GQ)], scalar=ucol[:, bass.ds(k * BPS + b, 1)],
                        in1=mask[:, b // BPC, (b % BPC) * GQ:(b % BPC + 1) * GQ], op0=ALU.max, op1=ALU.min,
                    ).then_inc(s_wts, 1)

            EPI = 11

            def chain(g, n, ins):
                ins.then_inc(s_epi, 1)
                dve.wait_ge(s_epi, EPI * g + n)

            def tiles(ap):
                return ap.rearrange("p (t d) -> p t d", d=D)

            def wide(ap):
                return ap.unsqueeze(2).to_broadcast([P, T, D])

            def attend(g, par):
                A = acc[par]
                dve.wait_ge(s_used, NB * g + NB)
                chain(g, 1, nc.vector.tensor_scalar(lone[:, :], A[:, :, D], 0.0, None, ALU.is_equal))
                chain(g, 2, nc.vector.tensor_tensor(den[:, :], A[:, :, D], lone[:, :], ALU.add))
                chain(g, 3, nc.vector.reciprocal(rden[:, :], den[:, :]))
                nc.vector.tensor_tensor(tiles(y[:, :]), wh_mean[:, :].unsqueeze(1).to_broadcast([P, T, D]),
                                        wide(lone[:, :]), ALU.mult)
                ins = nc.vector.tensor_tensor(tiles(h[:, :]), A[:, :, 0:D], wide(rden[:, :]), ALU.mult)
                chain(g, 4, ins)
                chain(g, 5, nc.vector.tensor_tensor(h[:, :], h[:, :], y[:, :], ALU.add))
                nc.vector.tensor_scalar(neg[:, :], h[:, :], 0.0, None, ALU.min).then_inc(s_neg, 1)

            def residual(g, par, turn):
                dve.wait_ge(s_exp, g + 1)
                chain(g, 6, nc.vector.scalar_tensor_tensor(out=y[:, :], in0=h[:, :], scalar=0.0, in1=neg[:, :],
                                                           op0=ALU.max, op1=ALU.add))
                dve.wait_ge(s_xr[par], 16 * turn + 16)
                ins = nc.vector.scalar_tensor_tensor(out=y[:, :], in0=y[:, :], scalar=-1.0, in1=x_res[:, par, :],
                                                     op0=ALU.add, op1=ALU.add)
                chain(g, 7, ins)
                for t in range(T):
                    last = nc.vector.bn_stats(stats[:, t, :], y[:, t * D:(t + 1) * D])
                chain(g, 8, last)
                m_e, m_o, q_e, q_o = (stats[:, :, i] for i in (1, 4, 2, 5))
                nc.vector.tensor_tensor(msum[:, :], m_e, m_o, ALU.add)
                nc.vector.tensor_tensor(mdif[:, :], m_e, m_o, ALU.subtract)
                chain(g, 9, nc.vector.tensor_tensor(qsum[:, :], q_e, q_o, ALU.add))
                nc.vector.tensor_scalar(mean[:, :], msum[:, :], 0.5, None, ALU.mult)
                chain(g, 10, nc.vector.scalar_tensor_tensor(out=mdif[:, :], in0=mdif[:, :], scalar=0.25,
                                                            in1=mdif[:, :], op0=ALU.mult, op1=ALU.mult))
                nc.vector.scalar_tensor_tensor(out=var[:, :], in0=qsum[:, :], scalar=1.0 / D, in1=mdif[:, :],
                                               op0=ALU.mult, op1=ALU.add).then_inc(s_var, 1)

            def normalise(g, par, turn, first=False):
                dve.wait_ge(s_std, g + 1)
                chain(g, 11, nc.vector.reciprocal(rstd[:, :], std[:, :]))
                if not first:
                    dve.wait_ge(s_st[par], 16 * turn)
                for t in range(T):
                    last = nc.vector.tensor_scalar(o[:, par, t * D:(t + 1) * D], y[:, t * D:(t + 1) * D],
                                                   mean[:, t:t + 1], rstd[:, t:t + 1], ALU.subtract, ALU.mult)
                last.then_inc(s_o, 1)

            def group(g, par, turn, first=False):
                weights(g, 0)
                weights(g, 1)
                attend(g - 1, par)
                weights(g, 2)
                residual(g - 1, par, turn)
                weights(g, 3)
                normalise(g - 1, par, turn, first)
                with dve.Fori(4, SPG) as k:
                    weights(g, k)

            weights(0, 0, first=True)
            with dve.Fori(1, SPG) as k:
                weights(0, k)
            group(1, 0, 0, first=True)
            group(2, 1, 0, first=True)
            with dve.Fori(1, NG // 2 - 1) as gp:
                group(2 * gp + 1, 0, gp)
                group(2 * gp + 2, 1, gp)
            group(NG - 1, 0, NG // 2 - 1)
            attend(NG - 1, 1)
            residual(NG - 1, 1, NG // 2 - 1)
            normalise(NG - 1, 1, NG // 2 - 1)

        @block.tensor
        def _(pe):
            pe.wait_ge(s_w, 48)
            nc.tensor.matmul(acc[0][:, 0, 0:2], w_t[:, :], a_t[:, :], start=True, stop=True).then_inc(s_wa, 1)
            pe.wait_ge(s_wext, 1)
            for n in range(QUARTERS * CPQ):
                if n % CPQ == 0:
                    pe.wait_ge(s_xt[n // CPQ], 16)
                if n >= 2:
                    pe.wait_ge(s_whc, n - 1)
                for b in range(KPP):
                    c = (n * KPP + b) * P
                    last = nc.tensor.matmul(acc[0][:, KPP * (n % 2) + b, 0:E], x_t[:, c:c + P], w_ext[:, :],
                                            start=True, stop=True)
                last.then_inc(s_whp, 1)
                if n >= 4:
                    pe.wait_ge(s_qc, n - 3)
                nc.tensor.matmul(acc[1][:, 2 * (n % 4):2 * (n % 4) + 2, :].rearrange("p t c -> p (t c)"), wa2[:, :],
                                 x_t[:, n * QC:(n + 1) * QC], start=True, stop=True).then_inc(s_qp, 1)
            pe.wait_ge(s_xm, 1)
            pe.wait_ge(s_qc, QUARTERS * CPQ)
            nc.tensor.matmul(acc[1][:, 0, 0:D], xmean[:, :], w_ext[:, 0:D], start=True, stop=True).then_inc(s_mp, 1)

            def products(g, par, k, begin=False, end=False):
                s = SPG * g + k
                for b in range(BPS):
                    pe.wait_ge(s_wts, BPS * s + (b + 1))
                    for t in range(T):
                        last = nc.tensor.matmul(acc[par][:, t, 0:E], wts[:, b, t * P:(t + 1) * P],
                                                v_all[:, bass.ds(BPS * k + b, 1), :].rearrange("p o e -> p (o e)"),
                                                start=begin and b == 0 and t % 2 == 0,
                                                stop=end and b == BPS - 1, skip_group_check=True)
                    last.then_inc(s_used, 1)

            def group(g, par):
                products(g, par, 0, begin=True)
                with pe.Fori(1, SPG - 1) as k:
                    products(g, par, k)
                products(g, par, SPG - 1, end=True)

            pe.wait_ge(s_v, 1)
            products(0, 0, 0, begin=True)
            with pe.Fori(1, SPG - 1) as k:
                pe.wait_ge(s_v, k + 1)
                products(0, 0, k)
            pe.wait_ge(s_v, SPG)
            products(0, 0, SPG - 1, end=True)
            group(1, 1)
            with pe.Fori(1, NG // 2) as gp:
                for par in range(2):
                    pe.wait_ge(s_neg, 2 * gp + (par - 1))
                    group(2 * gp + par, par)


def kernel(x, adj, L0_gnn_W, L0_gnn_a):
    import numpy as np
    import concourse.bacc as bacc
    from concourse.bass_utils import run_bass_kernel_spmd

    x, adj, W, a = (np.asarray(v) for v in (x, adj, L0_gnn_W, L0_gnn_a))
    n, d = x.shape
    P, GQ, BPC = 128, 1024, 2
    adjT = adj.T.reshape(n // P // BPC, BPC, P, n // GQ, GQ).transpose(3, 0, 2, 1, 4)
    arrays = {
        "xT": np.ascontiguousarray(x.T),
        "x": np.ascontiguousarray(x),
        "adjT": np.ascontiguousarray(adjT).reshape(-1, P, BPC * GQ),
        "W": np.ascontiguousarray(W),
        "WT": np.ascontiguousarray(W.T),
        "a": np.ascontiguousarray(a.reshape(2, d).T),
    }
    nc = bacc.Bacc("TRN2", target_bir_lowering=False, num_devices=1)
    args = [nc.dram_tensor(k, v.shape, mybir.dt.from_np(v.dtype), kind="ExternalInput").ap()
            for k, v in arrays.items()]
    out = nc.dram_tensor("out", (n, d), mybir.dt.float32, kind="ExternalOutput").ap()
    build(nc, *args, out)
    return run_bass_kernel_spmd(nc, [arrays], core_ids=[0]).results[0]["out"]
```

```python
from contextlib import ExitStack

import concourse.bass as bass
from concourse import mybir


def build(nc, xT, x, adjT, W, WT, a, r_dram, out):
    F32, BF16, I32 = mybir.dt.float32, mybir.dt.bfloat16, mybir.dt.int32
    ALU, ACT, AX = mybir.AluOpType, mybir.ActivationFunctionType, mybir.AxisListType

    P = 128
    N, D = x.shape
    GQ = 1024
    NG = N // GQ
    T = GQ // P
    NB = N // P
    BPC = 2
    SLOTS = 4
    BPS = BPC * SLOTS
    SPG = NB // BPS
    STEPS = NG * SPG
    E = D + 1
    KPP = 4
    QUARTERS = 4
    XQ = N // QUARTERS
    PIECES = NB // KPP
    SLOPE = 0.8
    OPEN = 2.0 ** 96
    LIMIT = 2.0 ** 95
    EPS = 1e-5

    ctx = ExitStack()
    with ctx:
        def sb(name, shape, dt=F32):
            return ctx.enter_context(nc.sbuf_tensor(name, shape, dt))

        def sem(name):
            return ctx.enter_context(nc.semaphore(name))

        w_ext = sb("w_ext", [P, D + 2])
        w_t = sb("w_t", [P, D])
        a_t = sb("a_t", [P, 2])
        ident = sb("ident", [P, P])
        r_all = sb("r_all", [P, N])
        v_all = sb("v_all", [P, NB, D + 2])
        cols = sb("cols", [P, 3, NB])
        bcol, ucol, rcol = (cols[:, i, :] for i in range(3))
        r_rows = sb("r_rows", [NB, P])
        kmax_p = sb("kmax_p", [P, 1])
        kmax = sb("kmax", [P, 1])
        xsum_q = sb("xsum_q", [P, QUARTERS])
        xsum = sb("xsum", [P, 1])
        xmean = sb("xmean", [P, P])
        wh_mean = sb("wh_mean", [P, D])
        eps = sb("eps", [P, 1])
        adj = sb("adj", [P, SLOTS, BPC * GQ], I32)
        mask = sb("mask", [P, SLOTS, BPC * GQ], BF16)
        wts = sb("wts", [P, BPS, GQ])
        x_t = wts[:, :, :].rearrange("p b q -> p (b q)")
        x_res = sb("x_res", [P, 2, GQ])
        h = sb("h", [P, GQ])
        neg = sb("neg", [P, GQ])
        y = sb("y", [P, GQ])
        o = sb("o", [P, 2, GQ])
        den = sb("den", [P, T])
        lone = sb("lone", [P, T])
        rden = sb("rden", [P, T])
        stats = sb("stats", [P, T, 6])
        msum = sb("msum", [P, T])
        mdif = sb("mdif", [P, T])
        qsum = sb("qsum", [P, T])
        mean = sb("mean", [P, T])
        var = sb("var", [P, T])
        std = sb("std", [P, T])
        rstd = sb("rstd", [P, T])
        acc = [ctx.enter_context(nc.psum_tensor(f"acc{i}", [P, T, 256], F32)) for i in range(2)]

        s_w = sem("weights_loaded")
        s_eps = sem("eps_ready")
        s_xt = [sem(f"xT_loaded{i}") for i in range(QUARTERS)]
        s_adj = [sem(f"adj_loaded{i}") for i in range(SLOTS)]
        s_wa = sem("wa_in_psum")
        s_wext = sem("w_ext_ready")
        s_whp = sem("wh_piece_in_psum")
        s_whc = sem("wh_piece_copied")
        s_id = sem("identity_steps")
        s_xs = sem("xT_quarter_summed")
        s_kp = sem("kmax_of_partitions")
        s_km = sem("kmax_ready")
        s_kc = sem("exponents_ready")
        s_one = sem("ones_column_ready")
        s_bu = sem("b_and_u_ready")
        s_rc = sem("r_column_ready")
        s_rp = sem("r_rows_in_psum")
        s_rr = sem("r_rows_ready")
        s_rd = sem("r_in_dram")
        s_r = [sem(f"r_broadcast{i}") for i in range(2)]
        s_v = sem("v_scaled")
        s_xm = sem("xmean_ready")
        s_mp = sem("wh_mean_in_psum")
        s_pre = sem("vector_prologue_steps")
        s_mask = sem("masks_ready")
        s_wts = sem("weight_tiles_ready")
        s_used = sem("weight_tiles_used")
        s_epi = sem("vector_epilogue_steps")
        s_neg = sem("neg_ready")
        s_exp = sem("exp_ready")
        s_var = sem("variance_ready")
        s_std = sem("std_ready")
        s_xr = [sem(f"x_res_loaded{i}") for i in range(2)]
        s_o = sem("out_tile_ready")
        s_st = [sem(f"out_stored{i}") for i in range(2)]

        def wh_piece(n):
            return acc[n // 2 % 2][:, KPP * (n % 2):KPP * (n % 2) + KPP, 0:D + 2]

        block = ctx.enter_context(nc.Block())

        @block.sync
        def _(sp):
            sp.dma_start(w_t[:, :], WT).then_inc(s_w, 16)
            sp.dma_start(a_t[:, :], a).then_inc(s_w, 16)
            sp.dma_start(w_ext[:, 0:D], W).then_inc(s_w, 16)
            for i in range(QUARTERS):
                sp.dma_start(x_t[:, i * XQ:(i + 1) * XQ], xT[:, i * XQ:(i + 1) * XQ]).then_inc(s_xt[i], 16)
            for c in range(SLOTS):
                sp.dma_start(adj[:, c, :], adjT[c, :, :]).then_inc(s_adj[c], 16)
            sp.wait_ge(s_rr, 1)
            sp.dma_start(r_dram.rearrange("(b p) -> b p", p=P), r_rows[:, :]).then_inc(s_rd, 16)
            sp.wait_ge(s_rd, 16)
            for i, (lo, hi) in enumerate([(0, GQ), (GQ, N)]):
                sp.dma_start(r_all[:, lo:hi], r_dram[lo:hi].unsqueeze(0).to_broadcast([P, hi - lo]))\
                    .then_inc(s_r[i], 16)
            with sp.Fori(1, STEPS) as s:
                for c in range(SLOTS):
                    sp.wait_ge(s_mask, SLOTS * s + (c - SLOTS + 1))
                    sp.dma_start(adj[:, c, :], adjT[bass.ds(SLOTS * s + c, 1), :, :].rearrange("o p n -> (o p) n"))\
                        .then_inc(s_adj[c], 16)

        @block.gpsimd
        def _(pool):
            nc.gpsimd.memset(ident[:, :], 0.0).then_inc(s_id, 1)
            pool.wait_ge(s_id, 1)
            nc.gpsimd.affine_select(out=ident[:, :], in_=ident[:, :], compare_op=ALU.not_equal, fill=1.0, base=0,
                                    pattern=[[-1, P]], channel_multiplier=1).then_inc(s_id, 1)
            pool.wait_ge(s_kp, 1)
            nc.gpsimd.partition_all_reduce(kmax[:, :], kmax_p[:, :], P, bass.bass_isa.ReduceOp.max).then_inc(s_km, 1)
            pool.wait_ge(s_one, 1)
            pool.wait_ge(s_bu, 1)
            for s in range(SPG):
                v = v_all[:, s * BPS:(s + 1) * BPS, 0:E]
                nc.gpsimd.tensor_tensor(v, v, cols[:, 0, s * BPS:(s + 1) * BPS].unsqueeze(2).to_broadcast([P, BPS, E]),
                                        ALU.mult).then_inc(s_v, 1)

            xg = x.rearrange("(g t p) d -> g p t d", t=T, p=P)
            og = out.rearrange("(g t p) d -> g p t d", t=T, p=P)

            def load(par, g):
                pool.dma_start(x_res[:, par, :].rearrange("p (t d) -> p t d", d=D),
                               xg[bass.ds(g, 1), :, :, :].rearrange("o p t d -> (o p) t d")).then_inc(s_xr[par], 16)

            def store(par, g):
                pool.wait_ge(s_o, g + 1)
                pool.dma_start(og[bass.ds(g, 1), :, :, :].rearrange("o p t d -> (o p) t d"),
                               o[:, par, :].rearrange("p (t d) -> p t d", d=D)).then_inc(s_st[par], 16)

            load(0, 0)
            load(1, 1)
            with pool.Fori(0, NG // 2 - 1) as gp:
                for par in range(2):
                    store(par, 2 * gp + par)
                    pool.wait_ge(s_var, 2 * gp + (par + 1))
                    load(par, 2 * gp + (par + 2))
            for par in range(2):
                store(par, NG - 2 + par)
            for par in range(2):
                pool.wait_ge(s_st[par], 16 * (NG // 2))

        @block.scalar
        def _(act):
            act.wait_ge(s_eps, 1)
            nc.scalar.activation(std[:, 0:1], eps[:, :], ACT.Exp)
            for i in range(QUARTERS):
                act.wait_ge(s_xt[i], 16)
                nc.scalar.activation(mask[:, i, :], x_t[:, i * XQ:(i + 1) * XQ], ACT.Copy,
                                     accum_out=xsum_q[:, i:i + 1]).then_inc(s_xs, 1)

            def masks(s, first=False, slots=range(SLOTS)):
                for c in slots:
                    act.wait_ge(s_adj[c], 16 * s + 16)
                    if not first:
                        act.wait_ge(s_wts, BPS * s + (BPC * (c + 1) - BPS))
                    nc.scalar.activation(mask[:, c, :], adj[:, c, :], ACT.Relu, scale=OPEN).then_inc(s_mask, 1)

            def exp_part(g):
                act.wait_ge(s_neg, g + 1)
                nc.scalar.activation(neg[:, :], neg[:, :], ACT.Exp).then_inc(s_exp, 1)

            def std_part(g):
                act.wait_ge(s_var, g + 1)
                nc.scalar.activation(std[:, :], var[:, :], ACT.Sqrt, bias=eps[:, :]).then_inc(s_std, 1)

            act.wait_ge(s_xs, QUARTERS)
            masks(0, first=True, slots=range(2))
            act.wait_ge(s_kc, 1)
            nc.scalar.activation(cols[:, :, :], cols[:, :, :], ACT.Exp).then_inc(s_bu, 1)
            masks(0, first=True, slots=range(2, SLOTS))
            with act.Fori(1, SPG) as s:
                masks(s)
            with act.Fori(1, NG) as g:
                for k in range(3):
                    masks(SPG * g + k)
                exp_part(g - 1)
                masks(SPG * g + 3)
                std_part(g - 1)
                with act.Fori(4, SPG) as k:
                    masks(SPG * g + k)
            exp_part(NG - 1)
            std_part(NG - 1)

        @block.vector
        def _(dve):
            steps = [0]

            def after(ins):
                steps[0] += 1
                ins.then_inc(s_pre, 1)
                dve.wait_ge(s_pre, steps[0])

            nc.vector.memset(eps[:, :], EPS).then_inc(s_eps, 1)
            dve.wait_ge(s_w, 48)
            dve.wait_ge(s_wa, 1)
            nc.vector.tensor_copy(w_ext[:, D:D + 2], acc[0][:, 0, 0:2]).then_inc(s_wext, 1)
            for n in range(PIECES):
                dve.wait_ge(s_whp, n + 1)
                nc.vector.tensor_copy(v_all[:, n * KPP:(n + 1) * KPP, :], wh_piece(n)).then_inc(s_whc, 1)
            dve.wait_ge(s_whc, PIECES)
            nc.vector.reduce_max(kmax_p[:, :], v_all[:, :, D], AX.X).then_inc(s_kp, 1)
            dve.wait_ge(s_xs, QUARTERS)
            after(nc.vector.reduce_sum(xsum[:, :], xsum_q[:, :], AX.X))
            nc.vector.tensor_scalar(xmean[:, :], xsum[:, 0:1].to_broadcast([P, P]), 1.0 / N, None, ALU.mult)\
                .then_inc(s_xm, 1)
            dve.wait_ge(s_km, 1)
            nc.vector.tensor_scalar(bcol, v_all[:, :, D], kmax[:, 0:1], None, ALU.subtract)
            nc.vector.tensor_scalar(ucol, v_all[:, :, D], kmax[:, 0:1], -SLOPE, ALU.subtract, ALU.mult)
            nc.vector.tensor_scalar(rcol, v_all[:, :, D + 1], kmax[:, 0:1], SLOPE, ALU.add, ALU.mult)\
                .then_inc(s_kc, 1)
            dve.wait_ge(s_kc, 1)
            nc.vector.memset(v_all[:, :, D:E], 1.0).then_inc(s_one, 1)
            dve.wait_ge(s_bu, 1)
            nc.vector.tensor_scalar(cols[:, 1:3, :], cols[:, 1:3, :], LIMIT, None, ALU.min).then_inc(s_rc, 1)
            dve.wait_ge(s_rp, 1)
            nc.vector.tensor_copy(r_rows[:, :], acc[1][0:NB, T // 2, 0:P]).then_inc(s_rr, 1)
            dve.wait_ge(s_mp, 1)
            after(nc.vector.tensor_copy(wh_mean[:, :], acc[1][:, 0, 0:D]))

            def weights(g, k, first=False):
                s = SPG * g + k
                for b in range(BPS):
                    if b % BPC == 0:
                        dve.wait_ge(s_mask, SLOTS * s + (b // BPC + 1))
                    if not first:
                        dve.wait_ge(s_used, BPS * s + (b - BPS + 1))
                    nc.vector.scalar_tensor_tensor(
                        out=wts[:, b, :], in0=r_all[:, bass.ds(g * GQ, GQ)], scalar=ucol[:, bass.ds(k * BPS + b, 1)],
                        in1=mask[:, b // BPC, (b % BPC) * GQ:(b % BPC + 1) * GQ], op0=ALU.max, op1=ALU.min,
                    ).then_inc(s_wts, 1)

            EPI = 11

            def chain(g, n, ins):
                ins.then_inc(s_epi, 1)
                dve.wait_ge(s_epi, EPI * g + n)

            def tiles(ap):
                return ap.rearrange("p (t d) -> p t d", d=D)

            def wide(ap):
                return ap.unsqueeze(2).to_broadcast([P, T, D])

            def attend(g, par):
                A = acc[par]
                dve.wait_ge(s_used, NB * g + NB)
                chain(g, 1, nc.vector.tensor_scalar(lone[:, :], A[:, :, D], 0.0, None, ALU.is_equal))
                chain(g, 2, nc.vector.tensor_tensor(den[:, :], A[:, :, D], lone[:, :], ALU.add))
                chain(g, 3, nc.vector.reciprocal(rden[:, :], den[:, :]))
                nc.vector.tensor_tensor(tiles(y[:, :]), wh_mean[:, :].unsqueeze(1).to_broadcast([P, T, D]),
                                        wide(lone[:, :]), ALU.mult)
                ins = nc.vector.tensor_tensor(tiles(h[:, :]), A[:, :, 0:D], wide(rden[:, :]), ALU.mult)
                chain(g, 4, ins)
                chain(g, 5, nc.vector.tensor_tensor(h[:, :], h[:, :], y[:, :], ALU.add))
                nc.vector.tensor_scalar(neg[:, :], h[:, :], 0.0, None, ALU.min).then_inc(s_neg, 1)

            def residual(g, par, turn):
                dve.wait_ge(s_exp, g + 1)
                chain(g, 6, nc.vector.scalar_tensor_tensor(out=y[:, :], in0=h[:, :], scalar=0.0, in1=neg[:, :],
                                                           op0=ALU.max, op1=ALU.add))
                dve.wait_ge(s_xr[par], 16 * turn + 16)
                ins = nc.vector.scalar_tensor_tensor(out=y[:, :], in0=y[:, :], scalar=-1.0, in1=x_res[:, par, :],
                                                     op0=ALU.add, op1=ALU.add)
                chain(g, 7, ins)
                for t in range(T):
                    last = nc.vector.bn_stats(stats[:, t, :], y[:, t * D:(t + 1) * D])
                chain(g, 8, last)
                m_e, m_o, q_e, q_o = (stats[:, :, i] for i in (1, 4, 2, 5))
                nc.vector.tensor_tensor(msum[:, :], m_e, m_o, ALU.add)
                nc.vector.tensor_tensor(mdif[:, :], m_e, m_o, ALU.subtract)
                chain(g, 9, nc.vector.tensor_tensor(qsum[:, :], q_e, q_o, ALU.add))
                nc.vector.tensor_scalar(mean[:, :], msum[:, :], 0.5, None, ALU.mult)
                chain(g, 10, nc.vector.scalar_tensor_tensor(out=mdif[:, :], in0=mdif[:, :], scalar=0.25,
                                                            in1=mdif[:, :], op0=ALU.mult, op1=ALU.mult))
                nc.vector.scalar_tensor_tensor(out=var[:, :], in0=qsum[:, :], scalar=1.0 / D, in1=mdif[:, :],
                                               op0=ALU.mult, op1=ALU.add).then_inc(s_var, 1)

            def normalise(g, par, turn, first=False):
                dve.wait_ge(s_std, g + 1)
                chain(g, 11, nc.vector.reciprocal(rstd[:, :], std[:, :]))
                if not first:
                    dve.wait_ge(s_st[par], 16 * turn)
                for t in range(T):
                    last = nc.vector.tensor_scalar(o[:, par, t * D:(t + 1) * D], y[:, t * D:(t + 1) * D],
                                                   mean[:, t:t + 1], rstd[:, t:t + 1], ALU.subtract, ALU.mult)
                last.then_inc(s_o, 1)

            def group(g, par, turn, first=False):
                weights(g, 0)
                weights(g, 1)
                attend(g - 1, par)
                weights(g, 2)
                residual(g - 1, par, turn)
                weights(g, 3)
                normalise(g - 1, par, turn, first)
                with dve.Fori(4, SPG) as k:
                    weights(g, k)

            dve.wait_ge(s_r[0], 16)
            weights(0, 0, first=True)
            with dve.Fori(1, SPG) as k:
                weights(0, k)
            dve.wait_ge(s_r[1], 16)
            group(1, 0, 0, first=True)
            group(2, 1, 0, first=True)
            with dve.Fori(1, NG // 2 - 1) as gp:
                group(2 * gp + 1, 0, gp)
                group(2 * gp + 2, 1, gp)
            group(NG - 1, 0, NG // 2 - 1)
            attend(NG - 1, 1)
            residual(NG - 1, 1, NG // 2 - 1)
            normalise(NG - 1, 1, NG // 2 - 1)

        @block.tensor
        def _(pe):
            pe.wait_ge(s_w, 48)
            nc.tensor.matmul(acc[0][:, 0, 0:2], w_t[:, :], a_t[:, :], start=True, stop=True).then_inc(s_wa, 1)
            pe.wait_ge(s_wext, 1)
            for n in range(PIECES):
                if n % (PIECES // QUARTERS) == 0:
                    pe.wait_ge(s_xt[n // (PIECES // QUARTERS)], 16)
                if n >= 4:
                    pe.wait_ge(s_whc, n - 3)
                for b in range(KPP):
                    c = (n * KPP + b) * P
                    last = nc.tensor.matmul(wh_piece(n)[:, b, :], x_t[:, c:c + P], w_ext[:, :],
                                            start=True, stop=True)
                last.then_inc(s_whp, 1)
            pe.wait_ge(s_whc, PIECES)
            pe.wait_ge(s_xm, 1)
            nc.tensor.matmul(acc[1][:, 0, 0:D], xmean[:, :], w_ext[:, 0:D], start=True, stop=True).then_inc(s_mp, 1)
            pe.wait_ge(s_id, 2)
            pe.wait_ge(s_rc, 1)
            nc.tensor.matmul(acc[1][0:NB, T // 2, 0:P], rcol, ident[:, :], start=True, stop=True).then_inc(s_rp, 1)

            def products(g, par, k, begin=False, end=False):
                s = SPG * g + k
                for b in range(BPS):
                    pe.wait_ge(s_wts, BPS * s + (b + 1))
                    for t in range(T):
                        last = nc.tensor.matmul(acc[par][:, t, 0:E], wts[:, b, t * P:(t + 1) * P],
                                                v_all[:, bass.ds(BPS * k + b, 1), 0:E].rearrange("p o e -> p (o e)"),
                                                start=begin and b == 0 and t % 2 == 0,
                                                stop=end and b == BPS - 1, skip_group_check=True)
                    last.then_inc(s_used, 1)

            def group(g, par):
                products(g, par, 0, begin=True)
                with pe.Fori(1, SPG - 1) as k:
                    products(g, par, k)
                products(g, par, SPG - 1, end=True)

            pe.wait_ge(s_v, 1)
            products(0, 0, 0, begin=True)
            with pe.Fori(1, SPG - 1) as k:
                pe.wait_ge(s_v, k + 1)
                products(0, 0, k)
            pe.wait_ge(s_v, SPG)
            products(0, 0, SPG - 1, end=True)
            group(1, 1)
            with pe.Fori(1, NG // 2) as gp:
                for par in range(2):
                    pe.wait_ge(s_neg, 2 * gp + (par - 1))
                    group(2 * gp + par, par)


def kernel(x, adj, L0_gnn_W, L0_gnn_a):
    import numpy as np
    import concourse.bacc as bacc
    from concourse.bass_utils import run_bass_kernel_spmd

    x, adj, W, a = (np.asarray(v) for v in (x, adj, L0_gnn_W, L0_gnn_a))
    n, d = x.shape
    P, GQ, BPC = 128, 1024, 2
    adjT = adj.T.reshape(n // P // BPC, BPC, P, n // GQ, GQ).transpose(3, 0, 2, 1, 4)
    arrays = {
        "xT": np.ascontiguousarray(x.T),
        "x": np.ascontiguousarray(x),
        "adjT": np.ascontiguousarray(adjT).reshape(-1, P, BPC * GQ),
        "W": np.ascontiguousarray(W),
        "WT": np.ascontiguousarray(W.T),
        "a": np.ascontiguousarray(a.reshape(2, d).T),
    }
    nc = bacc.Bacc("TRN2", target_bir_lowering=False, num_devices=1)
    args = [nc.dram_tensor(k, v.shape, mybir.dt.from_np(v.dtype), kind="ExternalInput").ap()
            for k, v in arrays.items()]
    out = nc.dram_tensor("out", (n, d), mybir.dt.float32, kind="ExternalOutput").ap()
    r_dram = nc.dram_tensor("r_row", (n,), mybir.dt.float32, kind="Internal").ap()
    build(nc, *args, r_dram, out)
    return run_bass_kernel_spmd(nc, [arrays], core_ids=[0]).results[0]["out"]
```

```python
from contextlib import ExitStack

import concourse.bass as bass
from concourse import mybir


def build(nc, xT, x, adjT, W, WT, a, r_dram, out):
    F32, BF16, I32 = mybir.dt.float32, mybir.dt.bfloat16, mybir.dt.int32
    ALU, ACT, AX = mybir.AluOpType, mybir.ActivationFunctionType, mybir.AxisListType

    P = 128
    N, D = x.shape
    GQ = 1024
    NG = N // GQ
    T = GQ // P
    NB = N // P
    BPC = 2
    SLOTS = 4
    BPS = BPC * SLOTS
    SPG = NB // BPS
    STEPS = NG * SPG
    HQ = GQ // 2
    HT = T // 2
    HBPS = 2 * BPS
    HSPG = NB // HBPS
    E = D + 1
    KPP = 4
    XPARTS = 8
    XQ = N // XPARTS
    PIECES = NB // KPP
    SLOPE = 0.8
    OPEN = 2.0 ** 96
    LIMIT = 2.0 ** 95
    EPS = 1e-5

    ctx = ExitStack()
    with ctx:
        def sb(name, shape, dt=F32):
            return ctx.enter_context(nc.sbuf_tensor(name, shape, dt))

        def sem(name):
            return ctx.enter_context(nc.semaphore(name))

        w_ext = sb("w_ext", [P, D + 2])
        w_t = sb("w_t", [P, D])
        a_t = sb("a_t", [P, 2])
        ident = sb("ident", [P, P])
        r_all = sb("r_all", [P, N])
        v_all = sb("v_all", [P, NB, D + 2])
        cols = sb("cols", [P, 3, NB])
        bcol, ucol, rcol = (cols[:, i, :] for i in range(3))
        r_rows = sb("r_rows", [NB, P])
        kmax_p = sb("kmax_p", [P, 1])
        kmax = sb("kmax", [P, 1])
        xsum_q = sb("xsum_q", [P, XPARTS])
        xsum = sb("xsum", [P, 1])
        xmean = sb("xmean", [P, P])
        wh_mean = sb("wh_mean", [P, D])
        eps = sb("eps", [P, 1])
        adj = sb("adj", [P, SLOTS, BPC * GQ], I32)
        mask = sb("mask", [P, SLOTS, BPC * GQ], BF16)
        wts = sb("wts", [P, BPS, GQ])
        x_t = wts[:, :, :].rearrange("p b q -> p (b q)")
        x_res = sb("x_res", [P, 2, GQ])
        h = sb("h", [P, GQ])
        neg = sb("neg", [P, GQ])
        y = sb("y", [P, GQ])
        o = sb("o", [P, 2, GQ])
        den = sb("den", [P, T])
        lone = sb("lone", [P, T])
        rden = sb("rden", [P, T])
        stats = sb("stats", [P, T, 6])
        msum = sb("msum", [P, T])
        mdif = sb("mdif", [P, T])
        qsum = sb("qsum", [P, T])
        mean = sb("mean", [P, T])
        var = sb("var", [P, T])
        std = sb("std", [P, T])
        rstd = sb("rstd", [P, T])
        acc = [ctx.enter_context(nc.psum_tensor(f"acc{i}", [P, T, 256], F32)) for i in range(2)]

        s_w = sem("weights_loaded")
        s_eps = sem("eps_ready")
        s_xt = [sem(f"xT_loaded{i}") for i in range(XPARTS)]
        s_adj = [sem(f"adj_loaded{i}") for i in range(SLOTS)]
        s_wa = sem("wa_in_psum")
        s_wext = sem("w_ext_ready")
        s_whp = sem("wh_piece_in_psum")
        s_whc = sem("wh_piece_copied")
        s_id = sem("identity_steps")
        s_xs = sem("xT_part_summed")
        s_kp = sem("kmax_of_partitions")
        s_km = sem("kmax_ready")
        s_kc = sem("exponents_ready")
        s_one = sem("ones_column_ready")
        s_bu = sem("b_and_u_ready")
        s_rc = sem("r_column_ready")
        s_rp = sem("r_rows_in_psum")
        s_rr = sem("r_rows_ready")
        s_rd = sem("r_in_dram")
        s_r = [sem(f"r_broadcast{i}") for i in range(2)]
        s_v = sem("v_scaled")
        s_xm = sem("xmean_ready")
        s_mp = sem("wh_mean_in_psum")
        s_pre = sem("vector_prologue_steps")
        s_mask = sem("masks_ready")
        s_wts = sem("weight_tiles_ready")
        s_used = sem("weight_tiles_used")
        s_epi = sem("vector_epilogue_steps")
        s_neg = sem("neg_ready")
        s_exp = sem("exp_ready")
        s_var = sem("variance_ready")
        s_std = sem("std_ready")
        s_xr = [sem(f"x_res_loaded{i}") for i in range(2)]
        s_o = sem("out_tile_ready")
        s_st = [sem(f"out_stored{i}") for i in range(2)]

        def wh_piece(n):
            return acc[n // 2 % 2][:, KPP * (n % 2):KPP * (n % 2) + KPP, 0:D + 2]

        block = ctx.enter_context(nc.Block())

        @block.sync
        def _(sp):
            sp.dma_start(w_t[:, :], WT).then_inc(s_w, 16)
            sp.dma_start(a_t[:, :], a).then_inc(s_w, 16)
            sp.dma_start(w_ext[:, 0:D], W).then_inc(s_w, 16)
            for i in range(XPARTS):
                sp.dma_start(x_t[:, i * XQ:(i + 1) * XQ], xT[:, i * XQ:(i + 1) * XQ]).then_inc(s_xt[i], 16)
            for c in range(SLOTS):
                sp.dma_start(adj[:, c, :], adjT[c, :, :]).then_inc(s_adj[c], 16)
            sp.wait_ge(s_rr, 1)
            sp.dma_start(r_dram.rearrange("(b p) -> b p", p=P), r_rows[:, :]).then_inc(s_rd, 16)
            sp.wait_ge(s_rd, 16)
            for i, (lo, hi) in enumerate([(0, GQ), (GQ, N)]):
                sp.dma_start(r_all[:, lo:hi], r_dram[lo:hi].unsqueeze(0).to_broadcast([P, hi - lo]))\
                    .then_inc(s_r[i], 16)
            with sp.Fori(1, STEPS) as s:
                for c in range(SLOTS):
                    sp.wait_ge(s_mask, SLOTS * s + (c - SLOTS + 1))
                    sp.dma_start(adj[:, c, :], adjT[bass.ds(SLOTS * s + c, 1), :, :].rearrange("o p n -> (o p) n"))\
                        .then_inc(s_adj[c], 16)

        @block.gpsimd
        def _(pool):
            nc.gpsimd.memset(ident[:, :], 0.0).then_inc(s_id, 1)
            pool.wait_ge(s_id, 1)
            nc.gpsimd.affine_select(out=ident[:, :], in_=ident[:, :], compare_op=ALU.not_equal, fill=1.0, base=0,
                                    pattern=[[-1, P]], channel_multiplier=1).then_inc(s_id, 1)
            pool.wait_ge(s_kp, 1)
            nc.gpsimd.partition_all_reduce(kmax[:, :], kmax_p[:, :], P, bass.bass_isa.ReduceOp.max).then_inc(s_km, 1)
            pool.wait_ge(s_one, 1)
            pool.wait_ge(s_bu, 1)
            for s in range(SPG):
                v = v_all[:, s * BPS:(s + 1) * BPS, 0:E]
                nc.gpsimd.tensor_tensor(v, v, cols[:, 0, s * BPS:(s + 1) * BPS].unsqueeze(2).to_broadcast([P, BPS, E]),
                                        ALU.mult).then_inc(s_v, 1)

            xg = x.rearrange("(g t p) d -> g p t d", t=T, p=P)
            og = out.rearrange("(g t p) d -> g p t d", t=T, p=P)

            def load(par, g):
                pool.dma_start(x_res[:, par, :].rearrange("p (t d) -> p t d", d=D),
                               xg[bass.ds(g, 1), :, :, :].rearrange("o p t d -> (o p) t d")).then_inc(s_xr[par], 16)

            def store(par, g):
                pool.wait_ge(s_o, g + 1)
                pool.dma_start(og[bass.ds(g, 1), :, :, :].rearrange("o p t d -> (o p) t d"),
                               o[:, par, :].rearrange("p (t d) -> p t d", d=D)).then_inc(s_st[par], 16)

            load(0, 0)
            load(1, 1)
            with pool.Fori(0, NG // 2 - 1) as gp:
                for par in range(2):
                    store(par, 2 * gp + par)
                    pool.wait_ge(s_var, 2 * gp + (par + 1))
                    load(par, 2 * gp + (par + 2))
            store(0, NG - 2)
            for half in range(2):
                pool.wait_ge(s_o, NG + half)
                pool.dma_start(og[NG - 1, :, half * HT:(half + 1) * HT, :],
                               o[:, 1, half * HQ:(half + 1) * HQ].rearrange("p (t d) -> p t d", d=D))\
                    .then_inc(s_st[1], 16)
            for par in range(2):
                pool.wait_ge(s_st[par], 16 * (NG // 2 + par))

        @block.scalar
        def _(act):
            act.wait_ge(s_eps, 1)
            nc.scalar.activation(std[:, 0:1], eps[:, :], ACT.Exp)
            for i in range(XPARTS):
                act.wait_ge(s_xt[i], 16)
                nc.scalar.activation(mask[:, :, :].rearrange("p c n -> p (c n)")[:, i * XQ:(i + 1) * XQ], x_t[:, i * XQ:(i + 1) * XQ], ACT.Copy,
                                     accum_out=xsum_q[:, i:i + 1]).then_inc(s_xs, 1)

            def masks(s, first=False, slots=range(SLOTS)):
                for c in slots:
                    act.wait_ge(s_adj[c], 16 * s + 16)
                    if not first:
                        act.wait_ge(s_wts, BPS * s + (BPC * (c + 1) - BPS))
                    nc.scalar.activation(mask[:, c, :], adj[:, c, :], ACT.Relu, scale=OPEN).then_inc(s_mask, 1)

            def exp_part(e, lo=0, hi=T):
                act.wait_ge(s_neg, e + 1)
                n = neg[:, lo * D:hi * D]
                nc.scalar.activation(n, n, ACT.Exp).then_inc(s_exp, 1)

            def std_part(e, lo=0, hi=T):
                act.wait_ge(s_var, e + 1)
                nc.scalar.activation(std[:, lo:hi], var[:, lo:hi], ACT.Sqrt, bias=eps[:, :]).then_inc(s_std, 1)

            act.wait_ge(s_xs, XPARTS)
            masks(0, first=True, slots=range(2))
            act.wait_ge(s_kc, 1)
            nc.scalar.activation(cols[:, :, :], cols[:, :, :], ACT.Exp).then_inc(s_bu, 1)
            masks(0, first=True, slots=range(2, SLOTS))
            with act.Fori(1, SPG) as s:
                masks(s)
            with act.Fori(1, NG - 1) as g:
                for k in range(3):
                    masks(SPG * g + k)
                exp_part(g - 1)
                masks(SPG * g + 3)
                std_part(g - 1)
                with act.Fori(4, SPG) as k:
                    masks(SPG * g + k)
            for half in range(2):
                s = SPG * (NG - 1) + HSPG * half
                tiles_before = ((0, T), (0, HT))[half]
                for k in range(3):
                    masks(s + k)
                exp_part(NG - 2 + half, *tiles_before)
                masks(s + 3)
                std_part(NG - 2 + half, *tiles_before)
            exp_part(NG, HT, T)
            std_part(NG, HT, T)

        @block.vector
        def _(dve):
            steps = [0]

            def after(ins):
                steps[0] += 1
                ins.then_inc(s_pre, 1)
                dve.wait_ge(s_pre, steps[0])

            nc.vector.memset(eps[:, :], EPS).then_inc(s_eps, 1)
            dve.wait_ge(s_w, 48)
            dve.wait_ge(s_wa, 1)
            nc.vector.tensor_copy(w_ext[:, D:D + 2], acc[0][:, 0, 0:2]).then_inc(s_wext, 1)
            for n in range(PIECES):
                dve.wait_ge(s_whp, n + 1)
                nc.vector.tensor_copy(v_all[:, n * KPP:(n + 1) * KPP, :], wh_piece(n)).then_inc(s_whc, 1)
            dve.wait_ge(s_whc, PIECES)
            nc.vector.reduce_max(kmax_p[:, :], v_all[:, :, D], AX.X).then_inc(s_kp, 1)
            dve.wait_ge(s_xs, XPARTS)
            after(nc.vector.reduce_sum(xsum[:, :], xsum_q[:, :], AX.X))
            nc.vector.tensor_scalar(xmean[:, :], xsum[:, 0:1].to_broadcast([P, P]), 1.0 / N, None, ALU.mult)\
                .then_inc(s_xm, 1)
            dve.wait_ge(s_km, 1)
            nc.vector.tensor_scalar(bcol, v_all[:, :, D], kmax[:, 0:1], None, ALU.subtract)
            nc.vector.tensor_scalar(ucol, v_all[:, :, D], kmax[:, 0:1], -SLOPE, ALU.subtract, ALU.mult)
            nc.vector.tensor_scalar(rcol, v_all[:, :, D + 1], kmax[:, 0:1], SLOPE, ALU.add, ALU.mult)\
                .then_inc(s_kc, 1)
            dve.wait_ge(s_kc, 1)
            nc.vector.memset(v_all[:, :, D:E], 1.0).then_inc(s_one, 1)
            dve.wait_ge(s_bu, 1)
            nc.vector.tensor_scalar(cols[:, 1:3, :], cols[:, 1:3, :], LIMIT, None, ALU.min).then_inc(s_rc, 1)
            dve.wait_ge(s_rp, 1)
            nc.vector.tensor_copy(r_rows[:, :], acc[1][0:NB, T // 2, 0:P]).then_inc(s_rr, 1)
            dve.wait_ge(s_mp, 1)
            after(nc.vector.tensor_copy(wh_mean[:, :], acc[1][:, 0, 0:D]))

            def weights(g, k, first=False):
                s = SPG * g + k
                for b in range(BPS):
                    if b % BPC == 0:
                        dve.wait_ge(s_mask, SLOTS * s + (b // BPC + 1))
                    if not first:
                        dve.wait_ge(s_used, BPS * s + (b - BPS + 1))
                    nc.vector.scalar_tensor_tensor(
                        out=wts[:, b, :], in0=r_all[:, bass.ds(g * GQ, GQ)], scalar=ucol[:, bass.ds(k * BPS + b, 1)],
                        in1=mask[:, b // BPC, (b % BPC) * GQ:(b % BPC + 1) * GQ], op0=ALU.max, op1=ALU.min,
                    ).then_inc(s_wts, 1)

            EPI = 11

            def chain(g, n, ins):
                ins.then_inc(s_epi, 1)
                dve.wait_ge(s_epi, EPI * g + n)

            def tiles(ap):
                return ap.rearrange("p (t d) -> p t d", d=D)

            def wide(ap):
                return ap.unsqueeze(2).to_broadcast([P, ap.shape[1], D])


            def attend(e, par, used, lo=0, hi=T):
                A, f = acc[par][:, lo:hi, :], slice(lo * D, hi * D)
                dve.wait_ge(s_used, used)
                chain(e, 1, nc.vector.tensor_scalar(lone[:, lo:hi], A[:, :, D], 0.0, None, ALU.is_equal))
                chain(e, 2, nc.vector.tensor_tensor(den[:, lo:hi], A[:, :, D], lone[:, lo:hi], ALU.add))
                chain(e, 3, nc.vector.reciprocal(rden[:, lo:hi], den[:, lo:hi]))
                nc.vector.tensor_tensor(tiles(y[:, f]), wh_mean[:, :].unsqueeze(1).to_broadcast([P, hi - lo, D]),
                                        wide(lone[:, lo:hi]), ALU.mult)
                chain(e, 4, nc.vector.tensor_tensor(tiles(h[:, f]), A[:, :, 0:D], wide(rden[:, lo:hi]), ALU.mult))
                chain(e, 5, nc.vector.tensor_tensor(h[:, f], h[:, f], y[:, f], ALU.add))
                nc.vector.tensor_scalar(neg[:, f], h[:, f], 0.0, None, ALU.min).then_inc(s_neg, 1)

            def residual(e, par, turn, lo=0, hi=T):
                f, t_ = slice(lo * D, hi * D), slice(lo, hi)
                dve.wait_ge(s_exp, e + 1)
                chain(e, 6, nc.vector.scalar_tensor_tensor(out=y[:, f], in0=h[:, f], scalar=0.0, in1=neg[:, f],
                                                           op0=ALU.max, op1=ALU.add))
                dve.wait_ge(s_xr[par], 16 * turn + 16)
                chain(e, 7, nc.vector.scalar_tensor_tensor(out=y[:, f], in0=y[:, f], scalar=-1.0,
                                                           in1=x_res[:, par, f], op0=ALU.add, op1=ALU.add))
                for t in range(lo, hi):
                    last = nc.vector.bn_stats(stats[:, t, :], y[:, t * D:(t + 1) * D])
                chain(e, 8, last)
                m_e, m_o, q_e, q_o = (stats[:, t_, i] for i in (1, 4, 2, 5))
                nc.vector.tensor_tensor(msum[:, t_], m_e, m_o, ALU.add)
                nc.vector.tensor_tensor(mdif[:, t_], m_e, m_o, ALU.subtract)
                chain(e, 9, nc.vector.tensor_tensor(qsum[:, t_], q_e, q_o, ALU.add))
                nc.vector.tensor_scalar(mean[:, t_], msum[:, t_], 0.5, None, ALU.mult)
                chain(e, 10, nc.vector.scalar_tensor_tensor(out=mdif[:, t_], in0=mdif[:, t_], scalar=0.25,
                                                            in1=mdif[:, t_], op0=ALU.mult, op1=ALU.mult))
                nc.vector.scalar_tensor_tensor(out=var[:, t_], in0=qsum[:, t_], scalar=1.0 / D, in1=mdif[:, t_],
                                               op0=ALU.mult, op1=ALU.add).then_inc(s_var, 1)

            def normalise(e, par, turn, first=False, lo=0, hi=T):
                dve.wait_ge(s_std, e + 1)
                chain(e, 11, nc.vector.reciprocal(rstd[:, lo:hi], std[:, lo:hi]))
                if not first:
                    dve.wait_ge(s_st[par], 16 * turn)
                for t in range(lo, hi):
                    last = nc.vector.tensor_scalar(o[:, par, t * D:(t + 1) * D], y[:, t * D:(t + 1) * D],
                                                   mean[:, t:t + 1], rstd[:, t:t + 1], ALU.subtract, ALU.mult)
                last.then_inc(s_o, 1)

            def group(g, par, turn, first=False):
                weights(g, 0)
                weights(g, 1)
                attend(g - 1, par, NB * g)
                weights(g, 2)
                residual(g - 1, par, turn)
                weights(g, 3)
                normalise(g - 1, par, turn, first)
                with dve.Fori(4, SPG) as k:
                    weights(g, k)

            dve.wait_ge(s_r[0], 16)
            weights(0, 0, first=True)
            with dve.Fori(1, SPG) as k:
                weights(0, k)
            dve.wait_ge(s_r[1], 16)
            group(1, 0, 0, first=True)
            group(2, 1, 0, first=True)
            with dve.Fori(1, NG // 2 - 1) as gp:
                group(2 * gp + 1, 0, gp)
                group(2 * gp + 2, 1, gp)

            def weights_half(half, k):
                s = SPG * (NG - 1) + HSPG * half + k
                q0 = (NG - 1) * GQ + half * HQ
                for b in range(BPS):
                    if b % BPC == 0:
                        dve.wait_ge(s_mask, SLOTS * s + (b // BPC + 1))
                    dve.wait_ge(s_used, BPS * s + (b - BPS + 1))
                    for i in range(2):
                        j, m = k * HBPS + 2 * b + i, 2 * (b % BPC) + i
                        last = nc.vector.scalar_tensor_tensor(
                            out=wts[:, b, i * HQ:(i + 1) * HQ], in0=r_all[:, q0:q0 + HQ], scalar=ucol[:, j:j + 1],
                            in1=mask[:, b // BPC, m * HQ:(m + 1) * HQ], op0=ALU.max, op1=ALU.min)
                    last.then_inc(s_wts, 1)

            for half in range(2):
                e, par, turn, (lo, hi) = NG - 2 + half, half, NG // 2 - 1, ((0, T), (0, HT))[half]
                weights_half(half, 0)
                weights_half(half, 1)
                attend(e, par, NB * (NG - 1) + half * BPS * HSPG, lo, hi)
                weights_half(half, 2)
                residual(e, par, turn, lo, hi)
                weights_half(half, 3)
                normalise(e, par, turn, lo=lo, hi=hi)
            attend(NG, 1, NB * NG, HT, T)
            residual(NG, 1, NG // 2 - 1, HT, T)
            normalise(NG, 1, NG // 2 - 1, lo=HT, hi=T)

        @block.tensor
        def _(pe):
            pe.wait_ge(s_w, 48)
            nc.tensor.matmul(acc[0][:, 0, 0:2], w_t[:, :], a_t[:, :], start=True, stop=True).then_inc(s_wa, 1)
            pe.wait_ge(s_wext, 1)
            for n in range(PIECES):
                if n % (PIECES // XPARTS) == 0:
                    pe.wait_ge(s_xt[n // (PIECES // XPARTS)], 16)
                if n >= 4:
                    pe.wait_ge(s_whc, n - 3)
                for b in range(KPP):
                    c = (n * KPP + b) * P
                    last = nc.tensor.matmul(wh_piece(n)[:, b, :], x_t[:, c:c + P], w_ext[:, :],
                                            start=True, stop=True)
                last.then_inc(s_whp, 1)
            pe.wait_ge(s_whc, PIECES)
            pe.wait_ge(s_xm, 1)
            nc.tensor.matmul(acc[1][:, 0, 0:D], xmean[:, :], w_ext[:, 0:D], start=True, stop=True).then_inc(s_mp, 1)
            pe.wait_ge(s_id, 2)
            pe.wait_ge(s_rc, 1)
            nc.tensor.matmul(acc[1][0:NB, T // 2, 0:P], rcol, ident[:, :], start=True, stop=True).then_inc(s_rp, 1)

            def products(g, par, k, begin=False, end=False):
                s = SPG * g + k
                for b in range(BPS):
                    pe.wait_ge(s_wts, BPS * s + (b + 1))
                    for t in range(T):
                        last = nc.tensor.matmul(acc[par][:, t, 0:E], wts[:, b, t * P:(t + 1) * P],
                                                v_all[:, bass.ds(BPS * k + b, 1), 0:E].rearrange("p o e -> p (o e)"),
                                                start=begin and b == 0 and t % 2 == 0,
                                                stop=end and b == BPS - 1, skip_group_check=True)
                    last.then_inc(s_used, 1)

            def group(g, par):
                products(g, par, 0, begin=True)
                with pe.Fori(1, SPG - 1) as k:
                    products(g, par, k)
                products(g, par, SPG - 1, end=True)

            pe.wait_ge(s_v, 1)
            products(0, 0, 0, begin=True)
            with pe.Fori(1, SPG - 1) as k:
                pe.wait_ge(s_v, k + 1)
                products(0, 0, k)
            pe.wait_ge(s_v, SPG)
            products(0, 0, SPG - 1, end=True)
            group(1, 1)
            with pe.Fori(1, NG // 2 - 1) as gp:
                for par in range(2):
                    pe.wait_ge(s_neg, 2 * gp + (par - 1))
                    group(2 * gp + par, par)
            pe.wait_ge(s_neg, NG - 3)
            group(NG - 2, 0)

            def products_half(half, k, begin=False, end=False):
                s = SPG * (NG - 1) + HSPG * half + k
                for b in range(BPS):
                    pe.wait_ge(s_wts, BPS * s + (b + 1))
                    for i in range(2):
                        for t in range(HT):
                            last = nc.tensor.matmul(
                                acc[1][:, HT * half + t, 0:E], wts[:, b, i * HQ + t * P:i * HQ + (t + 1) * P],
                                v_all[:, bass.ds(HBPS * k + 2 * b + i, 1), 0:E].rearrange("p o e -> p (o e)"),
                                start=begin and b == 0 and i == 0 and t % 2 == 0,
                                stop=end and b == BPS - 1 and i == 1, skip_group_check=True)
                    last.then_inc(s_used, 1)

            pe.wait_ge(s_neg, NG - 2)
            for half in range(2):
                products_half(half, 0, begin=True)
                with pe.Fori(1, HSPG - 1) as k:
                    products_half(half, k)
                products_half(half, HSPG - 1, end=True)


def kernel(x, adj, L0_gnn_W, L0_gnn_a):
    import numpy as np
    import concourse.bacc as bacc
    from concourse.bass_utils import run_bass_kernel_spmd

    x, adj, W, a = (np.asarray(v) for v in (x, adj, L0_gnn_W, L0_gnn_a))
    n, d = x.shape
    P = 128

    def chunks(adj, blocks, queries):
        a = adj.T.reshape(n // P // blocks, blocks, P, -1, queries).transpose(3, 0, 2, 1, 4)
        return a.reshape(-1, P, blocks * queries)

    GQ, BPC = 1024, 2
    adjT = np.concatenate([chunks(adj[:-GQ], BPC, GQ), chunks(adj[-GQ:], 2 * BPC, GQ // 2)])
    arrays = {
        "xT": np.ascontiguousarray(x.T),
        "x": np.ascontiguousarray(x),
        "adjT": adjT,
        "W": np.ascontiguousarray(W),
        "WT": np.ascontiguousarray(W.T),
        "a": np.ascontiguousarray(a.reshape(2, d).T),
    }
    nc = bacc.Bacc("TRN2", target_bir_lowering=False, num_devices=1)
    args = [nc.dram_tensor(k, v.shape, mybir.dt.from_np(v.dtype), kind="ExternalInput").ap()
            for k, v in arrays.items()]
    out = nc.dram_tensor("out", (n, d), mybir.dt.float32, kind="ExternalOutput").ap()
    r_dram = nc.dram_tensor("r_row", (n,), mybir.dt.float32, kind="Internal").ap()
    build(nc, *args, r_dram, out)
    return run_bass_kernel_spmd(nc, [arrays], core_ids=[0]).results[0]["out"]
```
